# Optimizing a Trainium2 kernel written in Bass

```python
import numpy as np
import jax
import jax.numpy as jnp

def _softmax(x, axis=-1):
    return jax.nn.softmax(x, axis=axis)
def _gelu(x):
    return jax.nn.gelu(x, approximate=True)
def _silu(x):
    return jax.nn.silu(x)
def _sigmoid(x):
    return jax.nn.sigmoid(x)
def _layernorm(x, axis=-1, eps=1e-5):
    m = jnp.mean(x, axis=axis, keepdims=True)
    v = jnp.var(x, axis=axis, keepdims=True)
    return (x - m) / jnp.sqrt(v + eps)
def _scatter_add(tgt, idx, src, axis=0):
    return tgt.at[idx].add(src)
def _segment_sum(src, seg, n):
    return jax.ops.segment_sum(src, seg, n)

kernel_name = 'mk_conv_seq_d1_conv_nchw256_70c581'

def setup_inputs(seed: int = 0):
    np.random.seed(seed)
    _w = jnp.asarray
    def _rec_inputs():
        import jax
        import jax.numpy as jnp
        _gk = jax.random.key(seed)
        x = -8.015e-05 + 0.9999 * jax.random.normal(jax.random.fold_in(_gk, 1), (8, 256, 160, 160), jnp.float32)
        return x
    x = _rec_inputs()
    def _L0_conv_setup():
        import jax, jax.numpy as jnp
        import numpy as np
        from jax import lax
        EPS = 1e-05

        def haar_dwt(x):
            B, C, H, W = x.shape
            xr = x.reshape(B, C, H // 2, 2, W // 2, 2)
            a = xr[:, :, :, 0, :, 0]
            b = xr[:, :, :, 0, :, 1]
            c = xr[:, :, :, 1, :, 0]
            d = xr[:, :, :, 1, :, 1]
            ll = (a + b + c + d) * 0.5
            lh = (a + b - c - d) * 0.5
            hl = (a - b + c - d) * 0.5
            hh = (a - b - c + d) * 0.5
            return (ll, lh, hl, hh)

        def haar_idwt(ll, lh, hl, hh):
            B, C, h, w = ll.shape
            a = (ll + lh + hl + hh) * 0.5
            b = (ll + lh - hl - hh) * 0.5
            c = (ll - lh + hl - hh) * 0.5
            d = (ll - lh - hl + hh) * 0.5
            out = jnp.stack([jnp.stack([a, b], axis=-1), jnp.stack([c, d], axis=-1)], axis=-2)
            out = out.transpose(0, 1, 2, 4, 3, 5).reshape(B, C, 2 * h, 2 * w)
            return out

        def conv1x1(x, w, b=None):
            y = jnp.einsum('oc,bchw->bohw', w, x)
            if b is not None:
                y = y + b[None, :, None, None]
            return y

        def bn_eval(x, g, b, m, v):
            inv = g * lax.rsqrt(v + EPS)
            return x * inv[None, :, None, None] + (b - m * inv)[None, :, None, None]
        key = jax.random.key(seed)
        ks = jax.random.split(key, 12)
        B, C, H, W = (8, 256, 160, 160)
        hid = C // 16
        f32 = jnp.float32
        x = jax.random.normal(ks[0], (B, C, H, W), f32)
        fusion_w = jax.random.normal(ks[1], (C, 4 * C), f32) * (1.0 / np.sqrt(4 * C))
        fusion_b = jnp.zeros((C,), f32)
        bn1_g = jnp.ones((C,), f32)
        bn1_b = jnp.zeros((C,), f32)
        bn1_m = jax.random.normal(ks[2], (C,), f32) * 0.1
        bn1_v = jax.random.uniform(ks[3], (C,), f32, 0.5, 1.5)
        sa_w = jax.random.normal(ks[4], (1, 2, 7, 7), f32) * (1.0 / np.sqrt(2 * 49))
        ca_w1 = jax.random.normal(ks[5], (hid, C), f32) * (1.0 / np.sqrt(C))
        ca_w2 = jax.random.normal(ks[6], (C, hid), f32) * (1.0 / np.sqrt(hid))
        proj_w = jax.random.normal(ks[7], (4 * C, C), f32) * (1.0 / np.sqrt(C))
        proj_b = jnp.zeros((4 * C,), f32)
        bn2_g = jnp.ones((4 * C,), f32)
        bn2_b = jnp.zeros((4 * C,), f32)
        bn2_m = jax.random.normal(ks[8], (4 * C,), f32) * 0.1
        bn2_v = jax.random.uniform(ks[9], (4 * C,), f32, 0.5, 1.5)
        return dict(x=x, fusion_w=fusion_w, fusion_b=fusion_b, bn1_g=bn1_g, bn1_b=bn1_b, bn1_m=bn1_m, bn1_v=bn1_v, sa_w=sa_w, ca_w1=ca_w1, ca_w2=ca_w2, proj_w=proj_w, proj_b=proj_b, bn2_g=bn2_g, bn2_b=bn2_b, bn2_m=bn2_m, bn2_v=bn2_v)
    _L0_conv_all = _L0_conv_setup()
    _L0_conv_in = {k: v for k, v in _L0_conv_all.items() if k in ('fusion_w', 'fusion_b', 'bn1_g', 'bn1_b', 'bn1_m', 'bn1_v', 'sa_w', 'ca_w1', 'ca_w2', 'proj_w', 'proj_b', 'bn2_g', 'bn2_b', 'bn2_m', 'bn2_v', )}
    del _L0_conv_all

    return {
        "x": x,
        "L0_conv_fusion_w": _L0_conv_in["fusion_w"],
        "L0_conv_fusion_b": _L0_conv_in["fusion_b"],
        "L0_conv_bn1_g": _L0_conv_in["bn1_g"],
        "L0_conv_bn1_b": _L0_conv_in["bn1_b"],
        "L0_conv_bn1_m": _L0_conv_in["bn1_m"],
        "L0_conv_bn1_v": _L0_conv_in["bn1_v"],
        "L0_conv_sa_w": _L0_conv_in["sa_w"],
        "L0_conv_ca_w1": _L0_conv_in["ca_w1"],
        "L0_conv_ca_w2": _L0_conv_in["ca_w2"],
        "L0_conv_proj_w": _L0_conv_in["proj_w"],
        "L0_conv_proj_b": _L0_conv_in["proj_b"],
        "L0_conv_bn2_g": _L0_conv_in["bn2_g"],
        "L0_conv_bn2_b": _L0_conv_in["bn2_b"],
        "L0_conv_bn2_m": _L0_conv_in["bn2_m"],
        "L0_conv_bn2_v": _L0_conv_in["bn2_v"],
    }

def reference(x, L0_conv_fusion_w, L0_conv_fusion_b, L0_conv_bn1_g, L0_conv_bn1_b, L0_conv_bn1_m, L0_conv_bn1_v, L0_conv_sa_w, L0_conv_ca_w1, L0_conv_ca_w2, L0_conv_proj_w, L0_conv_proj_b, L0_conv_bn2_g, L0_conv_bn2_b, L0_conv_bn2_m, L0_conv_bn2_v):
    import jax
    import jax.numpy as jnp
    def _L0_conv_ref(x, fusion_w, fusion_b, bn1_g, bn1_b, bn1_m, bn1_v, sa_w, ca_w1, ca_w2, proj_w, proj_b, bn2_g, bn2_b, bn2_m, bn2_v):
        import jax, jax.numpy as jnp
        import numpy as np
        from jax import lax
        EPS = 1e-05

        def haar_dwt(x):
            B, C, H, W = x.shape
            xr = x.reshape(B, C, H // 2, 2, W // 2, 2)
            a = xr[:, :, :, 0, :, 0]
            b = xr[:, :, :, 0, :, 1]
            c = xr[:, :, :, 1, :, 0]
            d = xr[:, :, :, 1, :, 1]
            ll = (a + b + c + d) * 0.5
            lh = (a + b - c - d) * 0.5
            hl = (a - b + c - d) * 0.5
            hh = (a - b - c + d) * 0.5
            return (ll, lh, hl, hh)

        def haar_idwt(ll, lh, hl, hh):
            B, C, h, w = ll.shape
            a = (ll + lh + hl + hh) * 0.5
            b = (ll + lh - hl - hh) * 0.5
            c = (ll - lh + hl - hh) * 0.5
            d = (ll - lh - hl + hh) * 0.5
            out = jnp.stack([jnp.stack([a, b], axis=-1), jnp.stack([c, d], axis=-1)], axis=-2)
            out = out.transpose(0, 1, 2, 4, 3, 5).reshape(B, C, 2 * h, 2 * w)
            return out

        def conv1x1(x, w, b=None):
            y = jnp.einsum('oc,bchw->bohw', w, x)
            if b is not None:
                y = y + b[None, :, None, None]
            return y

        def bn_eval(x, g, b, m, v):
            inv = g * lax.rsqrt(v + EPS)
            return x * inv[None, :, None, None] + (b - m * inv)[None, :, None, None]
        identity = x
        ll, lh, hl, hh = haar_dwt(x)
        wav = jnp.concatenate([ll, lh, hl, hh], axis=1)
        fused = jax.nn.relu(bn_eval(conv1x1(wav, fusion_w, fusion_b), bn1_g, bn1_b, bn1_m, bn1_v))
        avg_sp = jnp.mean(fused, axis=1, keepdims=True)
        max_sp = jnp.max(fused, axis=1, keepdims=True)
        sp_in = jnp.concatenate([avg_sp, max_sp], axis=1)
        sp_map = lax.conv_general_dilated(sp_in, sa_w, (1, 1), ((3, 3), (3, 3)), dimension_numbers=('NCHW', 'OIHW', 'NCHW'))
        spatial_out = jax.nn.sigmoid(sp_map) * fused
        avg_ch = jnp.mean(spatial_out, axis=(2, 3), keepdims=True)
        max_ch = jnp.max(spatial_out, axis=(2, 3), keepdims=True)

        def mlp(p):
            return conv1x1(jax.nn.relu(conv1x1(p, ca_w1)), ca_w2)
        ch_map = jax.nn.sigmoid(mlp(avg_ch) + mlp(max_ch))
        channel_out = ch_map * spatial_out
        projected = jax.nn.relu(bn_eval(conv1x1(channel_out, proj_w, proj_b), bn2_g, bn2_b, bn2_m, bn2_v))
        C = projected.shape[1] // 4
        ll_o = projected[:, :C]
        lh_o = projected[:, C:2 * C]
        hl_o = projected[:, 2 * C:3 * C]
        hh_o = projected[:, 3 * C:]
        reconstructed = haar_idwt(ll_o, lh_o, hl_o, hh_o)
        return reconstructed + identity

    def _gn(v, G=32, eps=1e-5):
        B_, C_, H_, W_ = v.shape
        g = v.reshape(B_, G, C_ // G, H_, W_)
        m = jnp.mean(g, axis=(2, 3, 4), keepdims=True)
        s = jnp.var(g, axis=(2, 3, 4), keepdims=True)
        return ((g - m) / jnp.sqrt(s + eps)).reshape(v.shape)

    def _ln_c(v, eps=1e-6):
        m = jnp.mean(v, axis=1, keepdims=True)
        s = jnp.var(v, axis=1, keepdims=True)
        return (v - m) / jnp.sqrt(s + eps)

    def _ln_t(v, eps=1e-5):
        m = jnp.mean(v, axis=-1, keepdims=True)
        s = jnp.var(v, axis=-1, keepdims=True)
        return (v - m) / jnp.sqrt(s + eps)

    def _to_tokens(v):
        B_, C_, H_, W_ = v.shape
        return v.reshape(B_, C_, H_ * W_).transpose(0, 2, 1)
    def _from_tokens(t, like):
        B_, C_, H_, W_ = like.shape
        return t.transpose(0, 2, 1).reshape(B_, C_, H_, W_)

    x = _L0_conv_ref(x, L0_conv_fusion_w, L0_conv_fusion_b, L0_conv_bn1_g, L0_conv_bn1_b, L0_conv_bn1_m, L0_conv_bn1_v, L0_conv_sa_w, L0_conv_ca_w1, L0_conv_ca_w2, L0_conv_proj_w, L0_conv_proj_b, L0_conv_bn2_g, L0_conv_bn2_b, L0_conv_bn2_m, L0_conv_bn2_v)
    return x


_drawn_inputs = setup_inputs


def setup_inputs(seed=0):
    import zlib

    import numpy as np

    out = dict(_drawn_inputs(seed))
    spreads = {'L0_conv_fusion_b': (0.0, 0.1),
     'L0_conv_bn1_g': (1.0, 0.2),
     'L0_conv_bn1_b': (0.0, 0.308),
     'L0_conv_proj_b': (0.0, 0.1),
     'L0_conv_bn2_g': (1.0, 0.2),
     'L0_conv_bn2_b': (0.0, 0.1)}
    factors = {}
    for name, (base, spread) in spreads.items():
        noise = np.random.default_rng([zlib.crc32(name.encode()), seed]).standard_normal(out[name].shape)
        drawn = base * np.exp(spread * noise) if base else spread * noise
        out[name] = jnp.asarray(drawn.astype(out[name].dtype))
    for name, factor in factors.items():
        out[name] = (out[name] * factor).astype(out[name].dtype)
    return out
```

```python
from contextlib import ExitStack

import concourse.bass as bass
from concourse import mybir

F32 = mybir.dt.float32
F32R = mybir.dt.float32r
BF16 = mybir.dt.bfloat16
ALU = mybir.AluOpType
ACT = mybir.ActivationFunctionType
AX = mybir.AxisListType

P = 128
EPS = 1e-5
ROWS = 5
LAG = 21
RING = 24
CHUNK = 4
STRAIGHT = 6


def haar_block(nc, x, fusion_w, fusion_b, bn1_g, bn1_b, bn1_m, bn1_v, sa_w, ca_w1, ca_w2,
               proj_w, proj_b, bn2_g, bn2_b, bn2_m, bn2_v, out):
    B, C, H, W = x.shape
    H2, W2 = H // 2, W // 2
    CT = C // P
    TILES = H2 // ROWS
    NT = B * TILES
    PX = ROWS * W2
    XP = 4 * PX
    NCH = TILES // CHUNK
    CPX = CHUNK * PX
    HID = ca_w1.shape[0]
    OC = proj_w.shape[0]
    NB = OC // P
    KS = sa_w.shape[2]
    PAD = KS // 2
    HP = H2 + 2 * PAD
    NK = 2 * KS
    assert C == 2 * P and H2 * W2 == TILES * PX and PX <= 512 and H2 <= P and W2 == H2
    assert TILES % CHUNK == 0 and RING % CHUNK == 0 and RING > LAG + 1 and LAG == TILES + 5

    x_v = x.rearrange("b (i p) h w -> b i p (h w)", p=P)
    out_v = out.rearrange("b (i p) h w -> b i p (h w)", p=P)
    sig_dram = nc.dram_tensor("sig_scratch", [1, H2 * W2], F32, kind="Internal").ap()

    with ExitStack() as ctx:
        def sb(name, shape, dt=F32):
            return ctx.enter_context(nc.sbuf_tensor(name, shape, dt))

        def sem(name):
            return ctx.enter_context(nc.semaphore(name))

        fused = sb("fused", [P, CT, RING * PX])
        xin = sb("xin", [P, 2, CT, XP])
        xre = sb("xre", [P, 2, CT, XP])
        wf = sb("wf", [P, CT, 4, C])
        wp_hi = sb("wp_hi", [P, CT, OC], F32R)
        wp_lo = sb("wp_lo", [P, CT, OC], F32R)
        y_hi = sb("y_hi", [P, 2, CT, PX], F32R)
        y_lo = sb("y_lo", [P, 2, CT, PX], F32R)
        relu = sb("relu", [P, 2, PX])
        sd = sb("sd", [P, 2, 2 * PX])
        cell = sb("cell", [P, XP])
        mx = sb("mx", [P, 2, PX])
        sm = sb("sm", [P, 2, PX])
        sigb = sb("sigb", [P, 2, CPX])
        junk = sb("junk", [P, CPX], BF16)
        maps = sb("maps", [W2, 2, HP])
        band = sb("band", [W2, NK, W2])
        sig = sb("sig", [H2, W2])
        ident = sb("ident", [P, P])
        ones = sb("ones", [P, 2])
        eye_pad = sb("eye_pad", [W2, W2 + 2 * PAD])
        taps = sb("taps", [W2, NK * KS])
        mlp_w = sb("mlp_w", [P, 4, P])
        v1 = sb("v1", [P, 5, CT])
        v2 = sb("v2", [P, 5, NB])
        t1 = sb("t1", [P, 4, CT + NB])
        bias1 = t1[:, 3, 0:CT]
        bias2 = t1[:, 3, CT:CT + NB]
        nbias2 = sb("nbias2", [P, NB])
        both = sb("both", [P, 2, CT])
        part = sb("part", [P, 2, CT, NCH])
        pool = sb("pool", [P, CT, 2])
        hid = sb("hid", [P, 2])
        logit = sb("logit", [P, CT])
        ch = sb("ch", [P, CT])

        stage = xre[:, :, :, :].rearrange("p a b c -> p (a b c)")
        fw = stage[:, 0:CT * 4 * C].rearrange("p (t q c) -> p t q c", t=CT, q=4)
        fh = stage[:, 8 * C:8 * C + CT * 4 * C].rearrange("p (t q c) -> p t q c", t=CT, q=4)
        pw = stage[:, 16 * C:16 * C + NB * C].rearrange("p (t c) -> p t c", t=NB)
        tmp = cell[:, 0:4 * C].rearrange("p (q c) -> p q c", q=4)
        tmp2 = sigb[:, :, :].rearrange("p a b -> p (a b)")[:, 0:4 * C].rearrange("p (q c) -> p q c", q=4)
        m1 = xin[:, 1, 0, 0:C]
        m2 = xin[:, 1, 1, 0:CT * P].rearrange("p (t h) -> p t h", t=CT)

        pp = [ctx.enter_context(nc.psum_tensor(f"pp{j}", [P, 512], F32)) for j in range(4)]
        pf = [ctx.enter_context(nc.psum_tensor(f"pf{j}", [P, 512], F32)) for j in range(2)]
        pm = ctx.enter_context(nc.psum_tensor("pm", [P, 1024], F32))
        MEANS = 640

        w_landed = sem("w_landed")
        v_landed = sem("v_landed")
        mlp_landed = sem("mlp_landed")
        taps_landed = sem("taps_landed")
        m_zero = sem("m_zero")
        ident_ready = sem("ident_ready")
        pool_mem = sem("pool_mem")
        ones_ready = sem("ones_ready")
        var_ready = sem("var_ready")
        root_ready = sem("root_ready")
        dve_step = sem("dve_step")
        fh_ready = sem("fh_ready")
        pw_ready = sem("pw_ready")
        wf_psum = sem("wf_psum")
        wf_ready = sem("wf_ready")
        wp_psum = sem("wp_psum")
        wphi_ready = sem("wphi_ready")
        wplo_ready = sem("wplo_ready")
        mlp_psum = sem("mlp_psum")
        mlp_ready = sem("mlp_ready")
        bias_ready = sem("bias_ready")
        band_pass = sem("band_pass")
        x_landed = [[sem(f"x_landed{p}{i}") for i in range(CT)] for p in range(2)]
        x_used0 = sem("x_used0")
        f_psum = sem("f_psum")
        f_ready = sem("f_ready")
        mx_ready = sem("mx_ready")
        sm_ready = sem("sm_ready")
        t_psum = sem("t_psum")
        map_ready = sem("map_ready")
        conv_psum = sem("conv_psum")
        sig_ready = sem("sig_ready")
        sig_stored = sem("sig_stored")
        sigb_landed = [sem(f"sigb_landed{p}") for p in range(2)]
        mult_done = sem("mult_done")
        cmax_done = sem("cmax_done")
        csum_done = sem("csum_done")
        pool_ready = sem("pool_ready")
        hid_psum = sem("hid_psum")
        hid_ready = sem("hid_ready")
        logit_psum = sem("logit_psum")
        logit_ready = sem("logit_ready")
        ch_ready = sem("ch_ready")
        hi_ready = sem("hi_ready")
        lo_ready = sem("lo_ready")
        p_psum = sem("p_psum")
        r_ready = sem("r_ready")
        sd_ready = sem("sd_ready")
        cell_ready = sem("cell_ready")
        add_done = sem("add_done")
        xre_landed = [[sem(f"xre_landed{p}{i}") for i in range(CT)] for p in range(2)]
        stored = [[sem(f"stored{p}{i}") for i in range(CT)] for p in range(2)]

        LL, LH, HL, HH = range(4)

        def need(eng, s, value):
            if isinstance(value, int) and value <= 0:
                return
            eng.wait_ge(s, value)

        class Slot:

            def __init__(self, n, h, u, first, last, t=None):
                self.n, self.h, self.u, self.t = n, h, u, t
                self.m = (TILES // 2) * n + h
                self.k = 2 * self.m + u
                self.a = last < NT
                self.turn = first >= 1 and last - 1 < NT
                self.c = first >= LAG
                self.c_next = first + 1 >= LAG and last + 1 - LAG < NT
                self.load_next = last + 1 < NT
                self.kc = self.k - LAG
                self.pc = 1 - u
                self.mc = self.m + (u - LAG) // 2
                self.kn = self.kc + 1
                self.pn = u
                self.mn = self.m + (u + 1 - LAG) // 2
                self.nb = n - 1
                self.mc_prev = self.m + (u - 1 - LAG) // 2
                self.c_is_first = first == LAG
                self.k_is_first = first + 1 == LAG
                self.b_is_first = first == TILES
                self.b = t if t is not None and t < 5 and first >= TILES and last < NT + TILES else None

            def tile(self, lag):
                t = 2 * self.h + self.u - lag
                if self.t is None:
                    return (self.n, t) if lag <= 1 else (self.n - 1, t + TILES)
                back = 0
                while t < 0:
                    t, back = t + TILES, back + 1
                while t >= TILES:
                    t, back = t - TILES, back - 1
                return self.n - back, t

        def slots(eng, body):
            def straight(n, ts, n_first=None, n_last=None):
                n_first, n_last = (n, n) if n_first is None else (n_first, n_last)
                for t in ts:
                    body(Slot(n, t // 2, t % 2, n_first * TILES + t, n_last * TILES + t, t))

            def looped(n, t0, n_first=None, n_last=None):
                n_first, n_last = (n, n) if n_first is None else (n_first, n_last)
                with eng.Fori(t0 // 2, TILES // 2 - 1) as h:
                    for u in range(2):
                        body(Slot(n, h, u, n_first * TILES + t0, n_last * TILES + TILES - 3))
                straight(n, range(TILES - 2, TILES), n_first, n_last)

            straight(0, range(2))
            looped(0, 2)
            straight(1, range(STRAIGHT))
            looped(1, STRAIGHT)
            with eng.Fori(2, B - 1) as n:
                straight(n, range(STRAIGHT), 2, B - 2)
                looped(n, STRAIGHT, 2, B - 2)
            for n in (B - 1, B):
                straight(n, range(STRAIGHT))
                looped(n, STRAIGHT)
            straight(B + 1, range(LAG - TILES))

        def ring(k, count=1):
            return bass.ds((k % RING) * PX, count * PX)

        block = ctx.enter_context(nc.Block())

        @block.sync
        def _(sp):
            sp.dma_start(fw, fusion_w.rearrange("(t p) (q c) -> p t q c", p=P, q=4)).then_inc(w_landed, 16)
            with nc.allow_non_contiguous_dma(reason="per-channel vectors"):
                for i, v in enumerate((fusion_b, bn1_g, bn1_b, bn1_m, bn1_v)):
                    sp.dma_start(v1[:, i, :], v.rearrange("(t p) -> p t", p=P)).then_inc(v_landed, 16)
            for i in range(CT):
                sp.dma_start(xin[:, 0, i, :], x_v[0, i, :, 0:XP]).then_inc(x_landed[0][i], 16)
            with nc.allow_non_contiguous_dma(reason="per-channel vectors"):
                for i, v in enumerate((proj_b, bn2_g, bn2_b, bn2_m, bn2_v)):
                    sp.dma_start(v2[:, i, :], v.rearrange("(t p) -> p t", p=P)).then_inc(v_landed, 16)
            sp.dma_start(pw, proj_w.rearrange("(t p) c -> p t c", p=P)).then_inc(w_landed, 16)
            sp.wait_ge(m_zero, 2)
            sp.dma_start(m1[0:HID, :], ca_w1).then_inc(mlp_landed, 16)
            with nc.allow_non_contiguous_dma(reason="short rows"):
                sp.dma_start(m2[:, :, 0:HID], ca_w2.rearrange("(t p) h -> p t h", p=P)).then_inc(mlp_landed, 16)
            sp.dma_start(taps[:, :], sa_w.rearrange("o m y x -> o (m y x)").to_broadcast([W2, NK * KS])
                         ).then_inc(taps_landed, 16)
            sp.wait_ge(mlp_psum, 1)

            def load_x(s, i):
                b, t = s.tile(-1)
                sp.dma_start(xin[:, 1 - s.u, i, :], x_v[b, i, :, bass.ds(t * XP, XP)]
                             ).then_inc(x_landed[1 - s.u][i], 16)

            def load_residual(s, i):
                b, t = s.tile(LAG - 1)
                need(sp, stored[s.pn][i], 16 * s.mn)
                sp.dma_start(xre[:, s.pn, i, :], x_v[b, i, :, bass.ds(t * XP, XP)]
                             ).then_inc(xre_landed[s.pn][i], 16)

            def store(lag, par, i, s, g):
                b, t = s.tile(lag)
                sp.wait_ge(add_done, g + 1)
                sp.dma_start(out_v[b, i, :, bass.ds(t * XP, XP)], xre[:, par, i, :]
                             ).then_inc(stored[par][i], 16)

            def load_sig(s, c):
                sp.dma_start(sigb[:, c % 2, :], sig_dram[:, c * CPX:(c + 1) * CPX].to_broadcast([P, CPX])
                             ).then_inc(sigb_landed[c % 2], 16)

            def body(s):
                if s.load_next:
                    need(sp, x_used0, s.k)
                    load_x(s, 0)
                    need(sp, f_psum, CT * s.k)
                    load_x(s, 1)
                if s.b == 1:
                    need(sp, mult_done, 2 * NCH * s.nb)
                    sp.wait_ge(sig_ready, s.nb + 1)
                    sp.dma_start(sig_dram.rearrange("o (h w) -> (o h) w", w=W2), sig[:, :]
                                 ).then_inc(sig_stored, 16)
                    sp.wait_ge(sig_stored, 16 * (s.nb + 1))
                    load_sig(s, 0)
                    load_sig(s, 1)
                if s.b in (2, 3):
                    sp.wait_ge(mult_done, 2 * NCH * s.nb + 2 * (s.b - 1))
                    load_sig(s, s.b)
                if s.c_next:
                    if s.k_is_first:
                        sp.wait_ge(wplo_ready, 4)
                        sp.wait_ge(wp_psum, 4)
                    load_residual(s, 0)
                if s.c and not s.c_is_first:
                    store(LAG + 1, s.pn, 1, s, 2 * s.kc - 1)
                if s.c:
                    store(LAG, s.pc, 0, s, 2 * s.kc)
                if s.c_next:
                    load_residual(s, 1)

            slots(sp, body)
            sp.wait_ge(add_done, 2 * NT)
            sp.dma_start(out_v[B - 1, 1, :, (TILES - 1) * XP:], xre[:, (NT - 1) % 2, 1, :]
                         ).then_inc(stored[(NT - 1) % 2][1], 16)
            for p in range(2):
                for i in range(CT):
                    sp.wait_ge(stored[p][i], 16 * (NT // 2))

        @block.gpsimd
        def _(gp):
            nc.gpsimd.memset(xin[:, 1, 0, 0:C], 0.0).then_inc(m_zero, 1)
            nc.gpsimd.memset(xin[:, 1, 1, 0:CT * P], 0.0).then_inc(m_zero, 1)
            nc.gpsimd.memset(ident[:, :], 0.0).then_inc(pool_mem, 1)
            nc.gpsimd.memset(eye_pad[:, :], 0.0).then_inc(pool_mem, 1)
            nc.gpsimd.memset(maps[:, :, :], 0.0).then_inc(ones_ready, 1)
            nc.gpsimd.memset(ones[:, :], 1.0).then_inc(ones_ready, 1)
            gp.wait_ge(pool_mem, 2)
            nc.gpsimd.affine_select(out=ident[:, :], in_=ident[:, :], compare_op=ALU.not_equal, fill=1.0,
                                    base=0, pattern=[[-1, P]], channel_multiplier=1).then_inc(ident_ready, 1)
            nc.gpsimd.affine_select(out=eye_pad[:, :], in_=eye_pad[:, :], compare_op=ALU.not_equal, fill=1.0,
                                    base=PAD, pattern=[[-1, W2 + 2 * PAD]], channel_multiplier=1
                                    ).then_inc(ident_ready, 1)

            def body(s):
                if s.turn:
                    gp.wait_ge(f_ready, CT * s.k)
                    need(gp, t_psum, s.k - 2)
                    par = 1 - s.u
                    f0 = fused[:, 0, ring(s.k - 1 + RING)]
                    f1 = fused[:, 1, ring(s.k - 1 + RING)]
                    nc.gpsimd.tensor_tensor(sm[:, par, :], f0, f1, ALU.add).then_inc(sm_ready, 1)
                for c in {1: (0,), 2: (1, 2), 3: (3,)}.get(s.b, ()):
                    gp.wait_ge(sigb_landed[c % 2], 16 * (2 * s.nb + c // 2 + 1))
                    for i in range(CT):
                        f = fused[:, i, ring(TILES * s.nb + CHUNK * c, CHUNK)]
                        nc.gpsimd.tensor_tensor(f, f, sigb[:, c % 2, :], ALU.mult).then_inc(mult_done, 1)

            slots(gp, body)

        @block.tensor
        def _(pe):
            pe.wait_ge(ident_ready, 1)
            pe.wait_ge(fh_ready, 8)
            for q in range(4):
                for i in range(CT):
                    for o in range(CT):
                        mm = pe.transpose(pp[q][:, (i * CT + o) * P:(i * CT + o + 1) * P],
                                          fh[:, o, q, i * P:(i + 1) * P], ident[:, :])
                mm.then_inc(wf_psum, 1)
            pe.wait_ge(pw_ready, 1)
            for q in range(4):
                bank = pf[q] if q < 2 else pm[:, (q - 2) * 512:(q - 1) * 512]
                for o in range(4):
                    mm = pe.transpose(bank[:, o * P:(o + 1) * P],
                                      pw[:, (q % 2) * 4 + o, (q // 2) * P:(q // 2 + 1) * P], ident[:, :])
                mm.then_inc(wp_psum, 1)
            pe.wait_ge(mlp_landed, 32)
            pe.wait_ge(wf_ready, 1)
            for i in range(CT):
                pe.transpose(pp[0][:, i * P:(i + 1) * P], m1[:, i * P:(i + 1) * P], ident[:, :])
            for i in range(CT):
                mm = pe.transpose(pp[0][:, (CT + i) * P:(CT + i + 1) * P], m2[:, i, :], ident[:, :])
            mm.then_inc(mlp_psum, 1)
            pe.wait_ge(wf_ready, 4)
            pe.wait_ge(wplo_ready, 4)
            pe.wait_ge(mlp_ready, 1)
            pe.wait_ge(ones_ready, 2)

            def project(s, i):
                g = 2 * s.kc + i
                for n, j in enumerate((LH, LL, HH, HL)):
                    if j in (LH, HH):
                        need(pe, r_ready, 2 * g - 1 + n // 2)
                    else:
                        need(pe, sd_ready, 4 * g - 2 + n - 1)
                    cols = slice(j * C + i * P, j * C + (i + 1) * P)
                    for kt in range(CT):
                        for m, (w, y) in enumerate(((wp_hi, y_hi), (wp_lo, y_hi), (wp_hi, y_lo))):
                            mm = pe.matmul(pp[j][:, 0:PX], w[:, kt, cols], y[:, s.pc, kt, :],
                                           start=(kt == 0 and m == 0), stop=(kt == CT - 1 and m == 2))
                    mm.then_inc(p_psum, 1)

            def fusion(s, i):
                pe.wait_ge(x_landed[s.u][i], 16 * (s.m + 1))
                xs = xin[:, s.u, i, :].rearrange("p (y r w s) -> p y r w s", r=2, w=W2, s=2)
                for q in range(4):
                    for o in range(CT):
                        if i == 0 and q == 0:
                            need(pe, f_ready, CT * (s.k - 1) + o + 1)
                        mm = pe.matmul(pf[o][:, 0:PX].rearrange("p (y w) -> p y w", w=W2),
                                       wf[:, i, q, o * P:(o + 1) * P], xs[:, :, q // 2, :, q % 2],
                                       start=(i == 0 and q == 0), stop=(i == CT - 1 and q == 3))
                        if i == 0 and q == 3 and o == CT - 1:
                            mm.then_inc(x_used0, 1)
                        if i == CT - 1 and q == 3:
                            mm.then_inc(f_psum, 1)

            def body(s):
                if s.a:
                    fusion(s, 0)
                if s.turn:
                    pe.wait_ge(mx_ready, s.k)
                    pe.wait_ge(sm_ready, s.k)
                    need(pe, map_ready, 2 * (s.k - 1))
                    if s.b == 1:
                        pe.wait_ge(sig_ready, s.nb + 1)
                    if s.t == 5:
                        need(pe, logit_ready, s.nb + 1)
                    par = 1 - s.u
                    for r in range(ROWS):
                        pe.transpose(pm[0:W2, r * P:(r + 1) * P], mx[:, par, r * W2:(r + 1) * W2], ident[:, :])
                    for r in range(ROWS):
                        mm = pe.matmul(pm[0:W2, MEANS + r:MEANS + r + 1], sm[:, par, r * W2:(r + 1) * W2],
                                       ones[:, 0:1], start=True, stop=True)
                    mm.then_inc(t_psum, 1)
                if s.c:
                    pe.wait_ge(lo_ready, CT * (s.kc + 1))
                    project(s, 0)
                if s.a:
                    fusion(s, 1)
                if s.b == 4:
                    pe.wait_ge(pool_ready, 2 * (s.nb + 1))
                    if s.turn:
                        pe.wait_ge(map_ready, 2 * s.k)
                    for i in range(CT):
                        mm = pe.matmul(pm[:, 0:2], mlp_w[:, i, :], pool[:, i, :],
                                       start=(i == 0), stop=(i == CT - 1))
                    mm.then_inc(hid_psum, 1)
                if s.c:
                    project(s, 1)
                if s.b == 0:
                    pe.wait_ge(map_ready, 2 * s.k)
                    if s.b_is_first:
                        pe.wait_ge(band_pass, KS * NK)
                    for j in range(NK):
                        mm = pe.matmul(pm[0:H2, 0:W2], maps[:, j // KS, j % KS:j % KS + H2], band[:, j, :],
                                       start=(j == 0), stop=(j == NK - 1))
                    mm.then_inc(conv_psum, 1)
                if s.b == 4:
                    pe.wait_ge(hid_ready, s.nb + 1)
                    for i in range(CT):
                        mm = pe.matmul(pm[:, 512 + 2 * i:514 + 2 * i], mlp_w[:, CT + i, :], hid[:, :],
                                       start=True, stop=True)
                    mm.then_inc(logit_psum, 1)

            slots(pe, body)

        @block.scalar
        def _(act):
            act.wait_ge(var_ready, 2)
            nc.scalar.activation(t1[:, 1, :], t1[:, 0, :], ACT.Sqrt).then_inc(root_ready, 1)
            for q in range(4):
                act.wait_ge(wf_psum, q + 1)
                nc.scalar.activation(wf[:, :, q, :], pp[q][:, :].rearrange("p (i o) -> p i o", i=CT),
                                     ACT.Copy).then_inc(wf_ready, 1)
            for q in range(4):
                act.wait_ge(wp_psum, q + 1)
                bank = pf[q][:, :] if q < 2 else pm[:, (q - 2) * 512:(q - 1) * 512]
                nc.scalar.activation(wp_hi[:, q // 2, (q % 2) * 512:(q % 2 + 1) * 512], bank,
                                     ACT.Copy).then_inc(wphi_ready, 1)
            act.wait_ge(mlp_psum, 1)
            nc.scalar.activation(mlp_w[:, :, :].rearrange("p a b -> p (a b)"), pp[0][:, :],
                                 ACT.Copy).then_inc(mlp_ready, 1)
            act.wait_ge(bias_ready, 3)

            def relus(s, i):
                g = 2 * s.kc + i
                for n, j in enumerate((LH, HH)):
                    act.wait_ge(p_psum, 4 * g + 1 + 2 * n)
                    need(act, sd_ready, 4 * g)
                    nc.scalar.activation(relu[:, n, :], pp[j][:, 0:PX], ACT.Relu,
                                         bias=bias2[:, j * CT + i:j * CT + i + 1]).then_inc(r_ready, 1)

            def upper(s):
                need(act, p_psum, 8 * s.kc)
                for i in range(CT):
                    nc.scalar.activation(y_hi[:, s.pn, i, :], fused[:, i, ring(s.kn + RING)], ACT.Copy,
                                         scale=ch[:, i:i + 1]).then_inc(hi_ready, 1)

            def body(s):
                if s.b == 1:
                    act.wait_ge(conv_psum, s.nb + 1)
                    need(act, sig_stored, 16 * s.nb)
                    nc.scalar.activation(sig[:, :], pm[0:H2, 0:W2], ACT.Sigmoid).then_inc(sig_ready, 1)
                if s.c:
                    relus(s, 0)
                if s.c_next and s.b != 4:
                    upper(s)
                for c in {2: (0,), 3: (1, 2), 4: (3,)}.get(s.b, ()):
                    act.wait_ge(mult_done, CT * (NCH * s.nb + c + 1))
                    need(act, pool_ready, 2 * s.nb)
                    for i in range(CT):
                        need(act, csum_done, CT * (NCH * s.nb + c) + i)
                        nc.scalar.activation(junk[:, :], fused[:, i, ring(TILES * s.nb + CHUNK * c, CHUNK)],
                                             ACT.Copy, scale=1.0 / (H2 * W2),
                                             accum_out=part[:, 0, i, c:c + 1]).then_inc(csum_done, 1)
                if s.b == 4:
                    act.wait_ge(hid_psum, s.nb + 1)
                    nc.scalar.activation(hid[:, :], pm[:, 0:2], ACT.Relu).then_inc(hid_ready, 1)
                if s.a:
                    for o in range(CT):
                        act.wait_ge(f_psum, CT * s.k + o + 1)
                        nc.scalar.activation(fused[:, o, ring(s.k)], pf[o][:, 0:PX], ACT.Relu,
                                             bias=bias1[:, o:o + 1]).then_inc(f_ready, 1)
                if s.c:
                    relus(s, 1)
                if s.b == 4:
                    act.wait_ge(logit_ready, s.nb + 1)
                    nc.scalar.activation(ch[:, :], logit[:, :], ACT.Sigmoid).then_inc(ch_ready, 1)
                    act.wait_ge(ch_ready, s.nb + 1)
                    upper(s)

            slots(act, body)

        @block.vector
        def _(dve):
            steps = [0]

            def link(ins):
                steps[0] += 1
                ins.then_inc(dve_step, 1)
                dve.wait_ge(dve_step, steps[0])

            dve.wait_ge(v_landed, 160)
            nc.vector.tensor_scalar(t1[:, 0, 0:CT], v1[:, 4, :], EPS, None, ALU.add).then_inc(var_ready, 1)
            nc.vector.tensor_scalar(t1[:, 0, CT:], v2[:, 4, :], EPS, None, ALU.add).then_inc(var_ready, 1)
            dve.wait_ge(var_ready, 2)
            dve.wait_ge(root_ready, 1)
            link(nc.vector.reciprocal(t1[:, 2, :], t1[:, 1, :]))
            link(nc.vector.tensor_tensor(t1[:, 2, :], t1[:, 2, :], t1[:, 0, :], ALU.mult))
            link(nc.vector.scalar_tensor_tensor(t1[:, 1, :], t1[:, 1, :], 0.0, t1[:, 2, :], ALU.add, ALU.add))
            link(nc.vector.tensor_scalar(t1[:, 1, :], t1[:, 1, :], 0.5, None, ALU.mult))
            link(nc.vector.reciprocal(t1[:, 2, :], t1[:, 1, :]))
            for v, cols in ((v1, slice(0, CT)), (v2, slice(CT, CT + NB))):
                link(nc.vector.tensor_tensor(t1[:, 2, cols], t1[:, 2, cols], v[:, 1, :], ALU.mult))
                link(nc.vector.tensor_tensor(t1[:, 3, cols], v[:, 0, :], v[:, 3, :], ALU.subtract))
                link(nc.vector.tensor_tensor(t1[:, 3, cols], t1[:, 3, cols], t1[:, 2, cols], ALU.mult))
                link(nc.vector.tensor_tensor(t1[:, 3, cols], t1[:, 3, cols], v[:, 2, :], ALU.add))
            link(nc.vector.tensor_scalar(t1[:, 2, :], t1[:, 2, :], 0.5, None, ALU.mult))

            dve.wait_ge(w_landed, 16)
            for o in range(CT):
                w = tmp if o == 0 else tmp2
                link(nc.vector.tensor_scalar(w[:, :, :], fw[:, o, :, :], t1[:, 2, o:o + 1], None, ALU.mult))
                for j in range(2):
                    nc.vector.tensor_tensor(fw[:, o, 2 * j, :], w[:, 2 * j, :], w[:, 2 * j + 1, :], ALU.add)
                    ins = nc.vector.tensor_tensor(fw[:, o, 2 * j + 1, :], w[:, 2 * j, :], w[:, 2 * j + 1, :],
                                                  ALU.subtract)
                link(ins)
                for r in range(2):
                    nc.vector.tensor_tensor(fh[:, o, 2 * r, :], fw[:, o, r, :], fw[:, o, 2 + r, :], ALU.add
                                            ).then_inc(fh_ready, 1)
                    ins = nc.vector.tensor_tensor(fh[:, o, 2 * r + 1, :], fw[:, o, r, :], fw[:, o, 2 + r, :],
                                                  ALU.subtract)
                    ins.then_inc(fh_ready, 1)

            dve.wait_ge(w_landed, 32)
            for t in range(NB):
                ins = nc.vector.tensor_scalar(pw[:, t, :], pw[:, t, :], t1[:, 2, CT + t:CT + t + 1], None, ALU.mult)
            ins.then_inc(pw_ready, 1)
            link(nc.vector.tensor_scalar(bias2, bias2, 0.5, None, ALU.mult))
            nc.vector.tensor_scalar(nbias2[:, :], bias2, -1.0, None, ALU.mult).then_inc(bias_ready, 1)
            ll, hl = bias2[:, LL * CT:LL * CT + CT], bias2[:, HL * CT:HL * CT + CT]
            nc.vector.tensor_tensor(both[:, 0, :], ll, hl, ALU.add).then_inc(bias_ready, 1)
            nc.vector.tensor_tensor(both[:, 1, :], ll, hl, ALU.subtract).then_inc(bias_ready, 1)
            dve.wait_ge(bias_ready, 3)
            for q in range(4):
                dve.wait_ge(wphi_ready, q + 1)
                bank = pf[q][:, :] if q < 2 else pm[:, (q - 2) * 512:(q - 1) * 512]
                cols = slice((q % 2) * 512, (q % 2 + 1) * 512)
                nc.vector.tensor_tensor(wp_lo[:, q // 2, cols], bank, wp_hi[:, q // 2, cols].bitcast(F32),
                                        ALU.subtract).then_inc(wplo_ready, 1)

            dve.wait_ge(taps_landed, 16)
            dve.wait_ge(ident_ready, 2)
            for dx in range(KS):
                if dx:
                    dve.wait_ge(band_pass, NK * dx)
                for j in range(NK):
                    tap = taps[:, j * KS + dx:j * KS + dx + 1]
                    eye = eye_pad[:, dx:dx + W2]
                    if dx == 0:
                        ins = nc.vector.tensor_scalar(band[:, j, :], eye, tap, None, ALU.mult)
                    else:
                        ins = nc.vector.scalar_tensor_tensor(band[:, j, :], eye, tap, band[:, j, :],
                                                             ALU.mult, ALU.add)
                    ins.then_inc(band_pass, 1)

            def butterflies(s, i):
                g = 2 * s.kc + i
                for n, j in enumerate((LL, HL)):
                    dve.wait_ge(p_psum, 4 * g + 2 + 2 * n)
                    dve.wait_ge(r_ready, 2 * g + 1 + n)
                    rows = sd[:, n, :].rearrange("p (y r w) -> p y r w", r=2, w=W2)
                    p = pp[j][:, 0:PX].rearrange("p (y w) -> p y w", w=W2)
                    q = relu[:, n, :].rearrange("p (y w) -> p y w", w=W2)
                    need(dve, cell_ready, 2 * g)
                    low = nbias2[:, j * CT + i:j * CT + i + 1]
                    nc.vector.scalar_tensor_tensor(rows[:, :, 0, :], p, low, q, ALU.max, ALU.add
                                                   ).then_inc(sd_ready, 1)
                    nc.vector.scalar_tensor_tensor(rows[:, :, 1, :], p, low, q, ALU.max, ALU.subtract
                                                   ).then_inc(sd_ready, 1)

            def cells(s, i):
                g = 2 * s.kc + i
                dve.wait_ge(sd_ready, 4 * (g + 1))
                need(dve, add_done, g)
                px = cell[:, :].rearrange("p (y w c) -> p y w c", w=W2, c=2)
                s0 = sd[:, 0, :].rearrange("p (y w) -> p y w", w=W2)
                s1 = sd[:, 1, :].rearrange("p (y w) -> p y w", w=W2)
                for c, op in enumerate((ALU.add, ALU.subtract)):
                    nc.vector.scalar_tensor_tensor(px[:, :, :, c], s0, both[:, c, i:i + 1], s1, ALU.add, op
                                                   ).then_inc(cell_ready, 1)

            def residual(mc, par, i, g):
                dve.wait_ge(xre_landed[par][i], 16 * (mc + 1))
                dve.wait_ge(cell_ready, 2 * (g + 1))
                nc.vector.tensor_tensor(xre[:, par, i, :], xre[:, par, i, :], cell[:, :], ALU.add
                                        ).then_inc(add_done, 1)

            def lower(s):
                dve.wait_ge(hi_ready, CT * (s.kn + 1))
                for i in range(CT):
                    nc.vector.scalar_tensor_tensor(y_lo[:, s.pn, i, :], fused[:, i, ring(s.kn + RING)],
                                                   ch[:, i:i + 1], y_hi[:, s.pn, i, :].bitcast(F32),
                                                   ALU.mult, ALU.subtract).then_inc(lo_ready, 1)

            def body(s):
                if s.turn:
                    dve.wait_ge(f_ready, CT * s.k)
                    need(dve, t_psum, s.k - 2)
                    nc.vector.tensor_tensor(mx[:, 1 - s.u, :], fused[:, 0, ring(s.k - 1 + RING)],
                                            fused[:, 1, ring(s.k - 1 + RING)], ALU.max).then_inc(mx_ready, 1)
                for c in {2: (0,), 3: (1, 2), 4: (3,)}.get(s.b, ()):
                    dve.wait_ge(mult_done, CT * (NCH * s.nb + c + 1))
                    nc.vector.tensor_reduce(part[:, 1, :, c], fused[:, :, ring(TILES * s.nb + CHUNK * c, CHUNK)],
                                            AX.X, ALU.max).then_inc(cmax_done, 1)
                if s.b == 4:
                    dve.wait_ge(csum_done, CT * NCH * (s.nb + 1))
                    dve.wait_ge(cmax_done, NCH * (s.nb + 1))
                    nc.vector.tensor_reduce(pool[:, :, 0], part[:, 0, :, :], AX.X, ALU.add).then_inc(pool_ready, 1)
                    nc.vector.tensor_reduce(pool[:, :, 1], part[:, 1, :, :], AX.X, ALU.max).then_inc(pool_ready, 1)
                if s.c:
                    butterflies(s, 0)
                    if not s.c_is_first:
                        residual(s.mc_prev, s.pn, 1, 2 * s.kc - 1)
                    cells(s, 0)
                if s.turn:
                    dve.wait_ge(t_psum, s.k)
                    _, t = s.tile(1)
                    nc.vector.tensor_reduce(maps[:, 1, bass.ds(t * ROWS + PAD, ROWS)],
                                            pm[0:W2, 0:ROWS * P].rearrange("p (r c) -> p r c", r=ROWS),
                                            AX.X, ALU.max).then_inc(map_ready, 1)
                    nc.vector.tensor_scalar(maps[:, 0, bass.ds(t * ROWS + PAD, ROWS)],
                                            pm[0:W2, MEANS:MEANS + ROWS], 1.0 / C, None, ALU.mult
                                            ).then_inc(map_ready, 1)
                if s.c_next and s.b != 4:
                    lower(s)
                if s.c:
                    butterflies(s, 1)
                    residual(s.mc, s.pc, 0, 2 * s.kc)
                    cells(s, 1)
                if s.b == 4:
                    dve.wait_ge(logit_psum, s.nb + 1)
                    nc.vector.tensor_reduce(logit[:, :], pm[:, 512:516].rearrange("p (i v) -> p i v", i=CT),
                                            AX.X, ALU.add).then_inc(logit_ready, 1)
                    lower(s)

            slots(dve, body)
            residual(NT // 2 - 1, (NT - 1) % 2, 1, 2 * NT - 1)


_INS = ["x"] + ["L0_conv_" + n for n in (
    "fusion_w", "fusion_b", "bn1_g", "bn1_b", "bn1_m", "bn1_v", "sa_w", "ca_w1", "ca_w2",
    "proj_w", "proj_b", "bn2_g", "bn2_b", "bn2_m", "bn2_v")]


def kernel(**inputs):
    import numpy as _np
    import concourse.bacc as _bacc
    from concourse import mybir as _mybir
    from concourse.bass_utils import run_bass_kernel_spmd as _run

    nc = _bacc.Bacc("TRN2", target_bir_lowering=False, num_devices=1, dynamic_dma_scratch_size=1024)
    arrays, args = {}, []
    for name in _INS:
        a = _np.ascontiguousarray(inputs[name])
        arrays[f"in_{name}_dram"] = a
        args.append(nc.dram_tensor(f"in_{name}_dram", a.shape, _mybir.dt.from_np(a.dtype), kind="ExternalInput").ap())
    shape = inputs["x"].shape
    args.append(nc.dram_tensor("out_0_dram", shape, _mybir.dt.float32, kind="ExternalOutput").ap())
    haar_block(nc, *args)
    r = _run(nc, [arrays], core_ids=[0])
    return r.results[0]["out_0_dram"]
```

```python
from contextlib import ExitStack

import concourse.bass as bass
from concourse import mybir

F32 = mybir.dt.float32
F32R = mybir.dt.float32r
BF16 = mybir.dt.bfloat16
ALU = mybir.AluOpType
ACT = mybir.ActivationFunctionType
AX = mybir.AxisListType

P = 128
EPS = 1e-5
ROWS = 5
LAG = 21
RING = 24
CHUNK = 2
STRAIGHT = 6


def haar_block(nc, x, fusion_w, fusion_b, bn1_g, bn1_b, bn1_m, bn1_v, sa_w, ca_w1, ca_w2,
               proj_w, proj_b, bn2_g, bn2_b, bn2_m, bn2_v, out):
    B, C, H, W = x.shape
    H2, W2 = H // 2, W // 2
    CT = C // P
    TILES = H2 // ROWS
    NT = B * TILES
    PX = ROWS * W2
    XP = 4 * PX
    NCH = TILES // CHUNK
    CPX = CHUNK * PX
    HID = ca_w1.shape[0]
    OC = proj_w.shape[0]
    NB = OC // P
    KS = sa_w.shape[2]
    PAD = KS // 2
    HP = H2 + 2 * PAD
    NK = 2 * KS
    assert C == 2 * P and H2 * W2 == TILES * PX and PX <= 512 and H2 <= P and W2 == H2
    assert KS == TILES // 2 - 1
    assert TILES % CHUNK == 0 and RING % CHUNK == 0 and RING > LAG + 1 and LAG == TILES + 5

    x_v = x.rearrange("b (i p) h w -> b i p (h w)", p=P)
    out_v = out.rearrange("b (i p) h w -> b i p (h w)", p=P)
    sig_dram = nc.dram_tensor("sig_scratch", [1, H2 * W2], F32, kind="Internal").ap()

    with ExitStack() as ctx:
        def sb(name, shape, dt=F32):
            return ctx.enter_context(nc.sbuf_tensor(name, shape, dt))

        def sem(name):
            return ctx.enter_context(nc.semaphore(name))

        fused = sb("fused", [P, CT, RING * PX])
        xin = sb("xin", [P, CT, XP])
        x_hi = sb("x_hi", [P, CT, XP], F32R)
        x_lo = sb("x_lo", [P, CT, XP], F32R)
        xre = sb("xre", [P, 2, CT, XP])
        wf_hi = sb("wf_hi", [P, CT, 4, C], F32R)
        wf_lo = sb("wf_lo", [P, CT, 4, C], F32R)
        wp_hi = sb("wp_hi", [P, CT, OC], F32R)
        wp_lo = sb("wp_lo", [P, CT, OC], F32R)
        y_hi = sb("y_hi", [P, 2, CT, PX], F32R)
        y_lo = sb("y_lo", [P, 2, CT, PX], F32R)
        relu = sb("relu", [P, 2, PX])
        sd = sb("sd", [P, 2, 2 * PX])
        cell = sb("cell", [P, XP])
        mx = sb("mx", [P, 2, PX])
        sm = sb("sm", [P, 2, PX])
        sigb = sb("sigb", [P, 2, CPX])
        junk = sb("junk", [P, CPX], BF16)
        maps = sb("maps", [W2, 2, HP])
        band = sb("band", [W2, NK, W2])
        sig = sb("sig", [H2, W2])
        ident = sb("ident", [P, P])
        ones = sb("ones", [P, 2])
        eye_pad = sb("eye_pad", [W2, W2 + 2 * PAD])
        taps = sb("taps", [W2, NK * KS])
        mlp_w = sb("mlp_w", [P, 4, P])
        v1 = sb("v1", [P, 5, CT])
        v2 = sb("v2", [P, 5, NB])
        t1 = sb("t1", [P, 4, CT + NB])
        bias1 = t1[:, 3, 0:CT]
        bias2 = t1[:, 3, CT:CT + NB]
        nbias2 = sb("nbias2", [P, NB])
        both = sb("both", [P, 2, CT])
        part = sb("part", [P, 2, CT, NCH])
        pool = sb("pool", [P, CT, 2])
        hid = sb("hid", [P, 2])
        logit = sb("logit", [P, CT])
        ch = sb("ch", [P, CT])

        stage = xre[:, :, :, :].rearrange("p a b c -> p (a b c)")
        fw = stage[:, 0:CT * 4 * C].rearrange("p (t q c) -> p t q c", t=CT, q=4)
        fh = stage[:, 8 * C:8 * C + CT * 4 * C].rearrange("p (t q c) -> p t q c", t=CT, q=4)
        pw = stage[:, 16 * C:16 * C + NB * C].rearrange("p (t c) -> p t c", t=NB)
        tmp = cell[:, 0:4 * C].rearrange("p (q c) -> p q c", q=4)
        tmp2 = sigb[:, :, :].rearrange("p a b -> p (a b)")[:, 0:4 * C].rearrange("p (q c) -> p q c", q=4)
        m1 = mx[:, 0, 0:C]
        m2 = mx[:, 1, 0:CT * P].rearrange("p (t h) -> p t h", t=CT)

        pp = [ctx.enter_context(nc.psum_tensor(f"pp{j}", [P, 512], F32)) for j in range(4)]
        pf = [ctx.enter_context(nc.psum_tensor(f"pf{j}", [P, 512], F32)) for j in range(2)]
        pm = ctx.enter_context(nc.psum_tensor("pm", [P, 1024], F32))
        MEANS = 640

        w_landed = sem("w_landed")
        v_landed = sem("v_landed")
        mlp_landed = sem("mlp_landed")
        taps_landed = sem("taps_landed")
        m_zero = sem("m_zero")
        ident_ready = sem("ident_ready")
        pool_mem = sem("pool_mem")
        ones_ready = sem("ones_ready")
        var_ready = sem("var_ready")
        root_ready = sem("root_ready")
        dve_step = sem("dve_step")
        fh_ready = sem("fh_ready")
        pw_ready = sem("pw_ready")
        wf_psum = sem("wf_psum")
        wfhi_ready = sem("wfhi_ready")
        wflo_ready = sem("wflo_ready")
        wp_psum = sem("wp_psum")
        wphi_ready = sem("wphi_ready")
        wplo_ready = sem("wplo_ready")
        mlp_psum = sem("mlp_psum")
        mlp_ready = sem("mlp_ready")
        bias_ready = sem("bias_ready")
        band_pass = sem("band_pass")
        x_landed = [sem(f"x_landed{i}") for i in range(CT)]
        xhi_ready = [sem(f"xhi_ready{i}") for i in range(CT)]
        xlo_ready = [sem(f"xlo_ready{i}") for i in range(CT)]
        x_used0 = sem("x_used0")
        f_psum = sem("f_psum")
        f_ready = sem("f_ready")
        mx_ready = sem("mx_ready")
        sm_ready = sem("sm_ready")
        t_psum = sem("t_psum")
        map_ready = sem("map_ready")
        conv_psum = sem("conv_psum")
        sig_ready = sem("sig_ready")
        sig_stored = sem("sig_stored")
        sigb_landed = [sem(f"sigb_landed{p}") for p in range(2)]
        mult_done = sem("mult_done")
        cmax_done = sem("cmax_done")
        csum_done = sem("csum_done")
        pool_ready = sem("pool_ready")
        hid_psum = sem("hid_psum")
        hid_ready = sem("hid_ready")
        logit_psum = sem("logit_psum")
        logit_ready = sem("logit_ready")
        ch_ready = sem("ch_ready")
        hi_ready = sem("hi_ready")
        lo_ready = sem("lo_ready")
        p_psum = sem("p_psum")
        r_ready = sem("r_ready")
        sd_ready = sem("sd_ready")
        cell_ready = sem("cell_ready")
        add_done = sem("add_done")
        xre_landed = [[sem(f"xre_landed{p}{i}") for i in range(CT)] for p in range(2)]
        stored = [[sem(f"stored{p}{i}") for i in range(CT)] for p in range(2)]

        LL, LH, HL, HH = range(4)

        def need(eng, s, value):
            if isinstance(value, int) and value <= 0:
                return
            eng.wait_ge(s, value)

        class Slot:

            def __init__(self, n, h, u, first, last, t=None):
                self.n, self.h, self.u, self.t = n, h, u, t
                self.m = (TILES // 2) * n + h
                self.k = 2 * self.m + u
                self.a = last < NT
                self.turn = first >= 1 and last - 1 < NT
                self.c = first >= LAG
                self.c_next = first + 1 >= LAG and last + 1 - LAG < NT
                self.load_next = last + 1 < NT
                self.load_second = last + 2 < NT
                self.kc = self.k - LAG
                self.pc = 1 - u
                self.mc = self.m + (u - LAG) // 2
                self.kn = self.kc + 1
                self.pn = u
                self.mn = self.m + (u + 1 - LAG) // 2
                self.nb = n - 1
                self.mc_prev = self.m + (u - 1 - LAG) // 2
                self.band_dx = 0 if first == 1 else h if t is None and first == 2 and u == 0 else None
                self.c_is_first = first == LAG
                self.pool_adds = first >= NT + 5
                self.pool_adds_prev = first > NT + 5
                self.k_is_first = first + 1 == LAG
                self.b_is_first = first == TILES
                self.b = t if t is not None and t < 5 and first >= TILES and last < NT + TILES else None
                self.after_b = t == 5 and first >= TILES and last < NT + TILES

            def tile(self, lag):
                t = 2 * self.h + self.u - lag
                if self.t is None:
                    return (self.n, t) if lag <= 1 else (self.n - 1, t + TILES)
                back = 0
                while t < 0:
                    t, back = t + TILES, back + 1
                while t >= TILES:
                    t, back = t - TILES, back - 1
                return self.n - back, t

        def slots(eng, body):
            def straight(n, ts, n_first=None, n_last=None):
                n_first, n_last = (n, n) if n_first is None else (n_first, n_last)
                for t in ts:
                    body(Slot(n, t // 2, t % 2, n_first * TILES + t, n_last * TILES + t, t))

            def looped(n, t0, n_first=None, n_last=None):
                n_first, n_last = (n, n) if n_first is None else (n_first, n_last)
                with eng.Fori(t0 // 2, TILES // 2 - 1) as h:
                    for u in range(2):
                        body(Slot(n, h, u, n_first * TILES + t0, n_last * TILES + TILES - 3))
                straight(n, range(TILES - 2, TILES), n_first, n_last)

            straight(0, range(2))
            looped(0, 2)
            straight(1, range(STRAIGHT))
            looped(1, STRAIGHT)
            with eng.Fori(2, B - 1) as n:
                straight(n, range(STRAIGHT), 2, B - 2)
                looped(n, STRAIGHT, 2, B - 2)
            for n in (B - 1, B):
                straight(n, range(STRAIGHT))
                looped(n, STRAIGHT)
            straight(B + 1, range(LAG - TILES))

        def ring(k, count=1):
            return bass.ds((k % RING) * PX, count * PX)

        def x_lower(eng, ops, k, i):
            eng.wait_ge(xhi_ready[i], k + 1)
            ops.tensor_tensor(x_lo[:, i, :], xin[:, i, :], x_hi[:, i, :].bitcast(F32), ALU.subtract
                              ).then_inc(xlo_ready[i], 1)

        def cells_of(s_adds, i):
            return xin[:, 1, :] if s_adds and i == 1 else cell[:, :]

        def residual(eng, ops, mc, par, i, g, px):
            eng.wait_ge(xre_landed[par][i], 16 * (mc + 1))
            eng.wait_ge(cell_ready, 2 * (g + 1))
            ops.tensor_tensor(xre[:, par, i, :], xre[:, par, i, :], px, ALU.add).then_inc(add_done, 1)

        block = ctx.enter_context(nc.Block())

        @block.sync
        def _(sp):
            sp.dma_start(fw, fusion_w.rearrange("(t p) (q c) -> p t q c", p=P, q=4)).then_inc(w_landed, 16)
            with nc.allow_non_contiguous_dma(reason="per-channel vectors"):
                for i, v in enumerate((fusion_b, bn1_g, bn1_b, bn1_m, bn1_v)):
                    sp.dma_start(v1[:, i, :], v.rearrange("(t p) -> p t", p=P)).then_inc(v_landed, 16)
            for i in range(CT):
                sp.dma_start(xin[:, i, :], x_v[0, i, :, 0:XP]).then_inc(x_landed[i], 16)
            with nc.allow_non_contiguous_dma(reason="per-channel vectors"):
                for i, v in enumerate((proj_b, bn2_g, bn2_b, bn2_m, bn2_v)):
                    sp.dma_start(v2[:, i, :], v.rearrange("(t p) -> p t", p=P)).then_inc(v_landed, 16)
            sp.dma_start(pw, proj_w.rearrange("(t p) c -> p t c", p=P)).then_inc(w_landed, 16)
            sp.wait_ge(m_zero, 2)
            sp.dma_start(m1[0:HID, :], ca_w1).then_inc(mlp_landed, 16)
            with nc.allow_non_contiguous_dma(reason="short rows"):
                sp.dma_start(m2[:, :, 0:HID], ca_w2.rearrange("(t p) h -> p t h", p=P)).then_inc(mlp_landed, 16)
            sp.dma_start(taps[:, :], sa_w.rearrange("o m y x -> o (m y x)").to_broadcast([W2, NK * KS])
                         ).then_inc(taps_landed, 16)

            def load_x(s, i, ahead):
                b, t = s.tile(-ahead)
                sp.wait_ge(xlo_ready[i], s.k + ahead)
                sp.dma_start(xin[:, i, :], x_v[b, i, :, bass.ds(t * XP, XP)]).then_inc(x_landed[i], 16)

            def load_residual(s, i):
                b, t = s.tile(LAG - 1)
                need(sp, stored[s.pn][i], 16 * s.mn)
                sp.dma_start(xre[:, s.pn, i, :], x_v[b, i, :, bass.ds(t * XP, XP)]
                             ).then_inc(xre_landed[s.pn][i], 16)

            def store(lag, par, i, s, g):
                b, t = s.tile(lag)
                sp.wait_ge(add_done, g + 1)
                sp.dma_start(out_v[b, i, :, bass.ds(t * XP, XP)], xre[:, par, i, :]
                             ).then_inc(stored[par][i], 16)

            def load_sig(s, c):
                sp.dma_start(sigb[:, c % 2, :], sig_dram[:, c * CPX:(c + 1) * CPX].to_broadcast([P, CPX])
                             ).then_inc(sigb_landed[c % 2], 16)

            def reload(s, c):
                if c is not None:
                    sp.wait_ge(mult_done, CT * (NCH * s.nb + c - 1))
                    load_sig(s, c)

            def body(s):
                if s.load_next:
                    load_x(s, 1, 1)
                if s.load_second:
                    load_x(s, 0, 2)
                if s.b == 1:
                    need(sp, mult_done, 2 * NCH * s.nb)
                    sp.wait_ge(sig_ready, s.nb + 1)
                    sp.dma_start(sig_dram.rearrange("o (h w) -> (o h) w", w=W2), sig[:, :]
                                 ).then_inc(sig_stored, 16)
                    sp.wait_ge(sig_stored, 16 * (s.nb + 1))
                    load_sig(s, 0)
                    load_sig(s, 1)
                if s.c_next:
                    if s.k_is_first:
                        sp.wait_ge(wplo_ready, 4)
                        sp.wait_ge(wp_psum, 4)
                    load_residual(s, 0)
                if s.c and not s.c_is_first:
                    store(LAG + 1, s.pn, 1, s, 2 * s.kc - 1)
                reload(s, {1: 2, 2: 4, 3: 6}.get(s.b))
                if s.c:
                    store(LAG, s.pc, 0, s, 2 * s.kc)
                reload(s, {1: 3, 2: 5, 3: 7}.get(s.b))
                if s.c_next:
                    load_residual(s, 1)

            sp.wait_ge(xlo_ready[0], 1)
            sp.dma_start(xin[:, 0, :], x_v[0, 0, :, XP:2 * XP]).then_inc(x_landed[0], 16)
            slots(sp, body)
            sp.wait_ge(add_done, 2 * NT)
            sp.dma_start(out_v[B - 1, 1, :, (TILES - 1) * XP:], xre[:, (NT - 1) % 2, 1, :]
                         ).then_inc(stored[(NT - 1) % 2][1], 16)
            for p in range(2):
                for i in range(CT):
                    sp.wait_ge(stored[p][i], 16 * (NT // 2))

        @block.gpsimd
        def _(gp):
            nc.gpsimd.memset(m1, 0.0).then_inc(m_zero, 1)
            nc.gpsimd.memset(mx[:, 1, 0:CT * P], 0.0).then_inc(m_zero, 1)
            nc.gpsimd.memset(ident[:, :], 0.0).then_inc(pool_mem, 1)
            nc.gpsimd.memset(eye_pad[:, :], 0.0).then_inc(pool_mem, 1)
            nc.gpsimd.memset(maps[:, :, :], 0.0).then_inc(ones_ready, 1)
            nc.gpsimd.memset(ones[:, :], 1.0).then_inc(ones_ready, 1)
            gp.wait_ge(pool_mem, 2)
            nc.gpsimd.affine_select(out=ident[:, :], in_=ident[:, :], compare_op=ALU.not_equal, fill=1.0,
                                    base=0, pattern=[[-1, P]], channel_multiplier=1).then_inc(ident_ready, 1)
            nc.gpsimd.affine_select(out=eye_pad[:, :], in_=eye_pad[:, :], compare_op=ALU.not_equal, fill=1.0,
                                    base=PAD, pattern=[[-1, W2 + 2 * PAD]], channel_multiplier=1
                                    ).then_inc(ident_ready, 1)

            def body(s):
                for c in {1: (0, 1), 2: (2, 3), 3: (4, 5), 4: (6, 7)}.get(s.b, ()):
                    gp.wait_ge(sigb_landed[c % 2], 16 * (NCH // 2 * s.nb + c // 2 + 1))
                    for i in range(CT):
                        f = fused[:, i, ring(TILES * s.nb + CHUNK * c, CHUNK)]
                        nc.gpsimd.tensor_tensor(f, f, sigb[:, c % 2, :], ALU.mult).then_inc(mult_done, 1)
                if s.a:
                    gp.wait_ge(f_ready, CT * (s.k + 1))
                    need(gp, t_psum, s.k - 1)
                    nc.gpsimd.tensor_tensor(sm[:, s.u, :], fused[:, 0, ring(s.k)], fused[:, 1, ring(s.k)],
                                            ALU.add).then_inc(sm_ready, 1)
                if s.load_next and s.c:
                    x_lower(gp, nc.gpsimd, s.k + 1, 1)
                if s.pool_adds_prev:
                    residual(gp, nc.gpsimd, s.mc_prev, s.pn, 1, 2 * s.kc - 1, cells_of(True, 1))
                if s.pool_adds:
                    residual(gp, nc.gpsimd, s.mc, s.pc, 0, 2 * s.kc, cells_of(True, 0))

            slots(gp, body)
            residual(gp, nc.gpsimd, NT // 2 - 1, (NT - 1) % 2, 1, 2 * NT - 1, cells_of(True, 1))

        @block.tensor
        def _(pe):
            pe.wait_ge(ident_ready, 1)
            pe.wait_ge(fh_ready, 8)
            for q in range(4):
                for i in range(CT):
                    for o in range(CT):
                        mm = pe.transpose(pp[q][:, (i * CT + o) * P:(i * CT + o + 1) * P],
                                          fh[:, o, q, i * P:(i + 1) * P], ident[:, :])
                mm.then_inc(wf_psum, 1)
            pe.wait_ge(pw_ready, 1)
            for q in range(4):
                bank = pf[q] if q < 2 else pm[:, (q - 2) * 512:(q - 1) * 512]
                for o in range(4):
                    mm = pe.transpose(bank[:, o * P:(o + 1) * P],
                                      pw[:, (q % 2) * 4 + o, (q // 2) * P:(q // 2 + 1) * P], ident[:, :])
                mm.then_inc(wp_psum, 1)
            pe.wait_ge(mlp_landed, 32)
            pe.wait_ge(wflo_ready, 1)
            for i in range(CT):
                pe.transpose(pp[0][:, i * P:(i + 1) * P], m1[:, i * P:(i + 1) * P], ident[:, :])
            for i in range(CT):
                mm = pe.transpose(pp[0][:, (CT + i) * P:(CT + i + 1) * P], m2[:, i, :], ident[:, :])
            mm.then_inc(mlp_psum, 1)
            pe.wait_ge(wflo_ready, 4)
            pe.wait_ge(wplo_ready, 4)
            pe.wait_ge(mlp_ready, 1)
            pe.wait_ge(ones_ready, 2)

            def project(s, i):
                g = 2 * s.kc + i
                for n, j in enumerate((LH, LL, HH, HL)):
                    if j in (LH, HH):
                        need(pe, r_ready, 2 * g - 1 + n // 2)
                    else:
                        need(pe, sd_ready, 4 * g - 2 + n - 1)
                    cols = slice(j * C + i * P, j * C + (i + 1) * P)
                    for kt in range(CT):
                        for m, (w, y) in enumerate(((wp_hi, y_hi), (wp_lo, y_hi), (wp_hi, y_lo))):
                            mm = pe.matmul(pp[j][:, 0:PX], w[:, kt, cols], y[:, s.pc, kt, :],
                                           start=(kt == 0 and m == 0), stop=(kt == CT - 1 and m == 2))
                    mm.then_inc(p_psum, 1)

            def fusion(s, i):
                pe.wait_ge(xlo_ready[i], s.k + 1)
                xh, xl = (v[:, i, :].rearrange("p (y r w s) -> p y r w s", r=2, w=W2, s=2) for v in (x_hi, x_lo))
                for q in range(4):
                    for o in range(CT):
                        if i == 0 and q == 0:
                            need(pe, f_ready, CT * (s.k - 1) + o + 1)
                        for m, (w, v) in enumerate(((wf_hi, xh), (wf_lo, xh), (wf_hi, xl))):
                            mm = pe.matmul(pf[o][:, 0:PX].rearrange("p (y w) -> p y w", w=W2),
                                           w[:, i, q, o * P:(o + 1) * P], v[:, :, q // 2, :, q % 2],
                                           start=(i == 0 and q == 0 and m == 0),
                                           stop=(i == CT - 1 and q == 3 and m == 2))
                        if i == 0 and q == 3 and o == CT - 1:
                            mm.then_inc(x_used0, 1)
                        if i == CT - 1 and q == 3:
                            mm.then_inc(f_psum, 1)

            def body(s):
                if s.a:
                    fusion(s, 0)
                if s.after_b:
                    pe.wait_ge(pool_ready, 2 * (s.nb + 1))
                    if s.turn:
                        pe.wait_ge(map_ready, 2 * (s.k - 1))
                    for i in range(CT):
                        mm = pe.matmul(pm[:, 0:2], mlp_w[:, i, :], pool[:, i, :],
                                       start=(i == 0), stop=(i == CT - 1))
                    mm.then_inc(hid_psum, 1)
                    pe.wait_ge(hid_ready, s.nb + 1)
                    for i in range(CT):
                        mm = pe.matmul(pm[:, 512 + 2 * i:514 + 2 * i], mlp_w[:, CT + i, :], hid[:, :],
                                       start=True, stop=True)
                    mm.then_inc(logit_psum, 1)
                    if s.a:
                        fusion(s, 1)
                if s.c:
                    pe.wait_ge(lo_ready, CT * (s.kc + 1))
                    project(s, 0)
                if s.turn:
                    pe.wait_ge(mx_ready, s.k)
                    pe.wait_ge(sm_ready, s.k)
                    need(pe, map_ready, 2 * (s.k - 1))
                    if s.b == 1:
                        pe.wait_ge(sig_ready, s.nb + 1)
                    if s.t == 5:
                        need(pe, logit_ready, s.nb + 1)
                    par = 1 - s.u
                    for r in range(ROWS):
                        pe.transpose(pm[0:W2, r * P:(r + 1) * P], mx[:, par, r * W2:(r + 1) * W2], ident[:, :])
                    for r in range(ROWS):
                        mm = pe.matmul(pm[0:W2, MEANS + r:MEANS + r + 1], sm[:, par, r * W2:(r + 1) * W2],
                                       ones[:, 0:1], start=True, stop=True)
                    mm.then_inc(t_psum, 1)
                if s.a and not s.after_b:
                    fusion(s, 1)
                if s.c:
                    project(s, 1)
                if s.b == 0:
                    pe.wait_ge(map_ready, 2 * s.k)
                    if s.b_is_first:
                        pe.wait_ge(band_pass, KS * NK)
                    for j in range(NK):
                        mm = pe.matmul(pm[0:H2, 0:W2], maps[:, j // KS, j % KS:j % KS + H2], band[:, j, :],
                                       start=(j == 0), stop=(j == NK - 1))
                    mm.then_inc(conv_psum, 1)

            slots(pe, body)

        @block.scalar
        def _(act):
            def x_upper(k, i):
                act.wait_ge(x_landed[i], 16 * (k + 1))
                need(act, *((x_used0, k) if i == 0 else (f_psum, CT * k)))
                nc.scalar.activation(x_hi[:, i, :], xin[:, i, :], ACT.Copy).then_inc(xhi_ready[i], 1)

            act.wait_ge(var_ready, 2)
            nc.scalar.activation(t1[:, 1, :], t1[:, 0, :], ACT.Sqrt).then_inc(root_ready, 1)
            for q in range(4):
                act.wait_ge(wf_psum, q + 1)
                nc.scalar.activation(wf_hi[:, :, q, :], pp[q][:, :].rearrange("p (i o) -> p i o", i=CT),
                                     ACT.Copy).then_inc(wfhi_ready, 1)
            for i in range(CT):
                x_upper(0, i)
            for q in range(4):
                act.wait_ge(wp_psum, q + 1)
                bank = pf[q][:, :] if q < 2 else pm[:, (q - 2) * 512:(q - 1) * 512]
                nc.scalar.activation(wp_hi[:, q // 2, (q % 2) * 512:(q % 2 + 1) * 512], bank,
                                     ACT.Copy).then_inc(wphi_ready, 1)
            act.wait_ge(mlp_psum, 1)
            nc.scalar.activation(mlp_w[:, :, :].rearrange("p a b -> p (a b)"), pp[0][:, :],
                                 ACT.Copy).then_inc(mlp_ready, 1)
            act.wait_ge(bias_ready, 3)

            def relus(s, i):
                g = 2 * s.kc + i
                for n, j in enumerate((LH, HH)):
                    act.wait_ge(p_psum, 4 * g + 1 + 2 * n)
                    need(act, sd_ready, 4 * g)
                    nc.scalar.activation(relu[:, n, :], pp[j][:, 0:PX], ACT.Relu,
                                         bias=bias2[:, j * CT + i:j * CT + i + 1]).then_inc(r_ready, 1)

            def chunk_means(s, c):
                act.wait_ge(mult_done, CT * (NCH * s.nb + c + 1))
                need(act, pool_ready, 2 * s.nb)
                for i in range(CT):
                    need(act, csum_done, CT * (NCH * s.nb + c) + i)
                    nc.scalar.activation(junk[:, :], fused[:, i, ring(TILES * s.nb + CHUNK * c, CHUNK)],
                                         ACT.Copy, scale=1.0 / (H2 * W2),
                                         accum_out=part[:, 0, i, c:c + 1]).then_inc(csum_done, 1)

            def upper(s):
                need(act, p_psum, 8 * s.kc)
                for i in range(CT):
                    nc.scalar.activation(y_hi[:, s.pn, i, :], fused[:, i, ring(s.kn + RING)], ACT.Copy,
                                         scale=ch[:, i:i + 1]).then_inc(hi_ready, 1)

            def body(s):
                if s.b == 1:
                    act.wait_ge(conv_psum, s.nb + 1)
                    need(act, sig_stored, 16 * s.nb)
                    nc.scalar.activation(sig[:, :], pm[0:H2, 0:W2], ACT.Sigmoid).then_inc(sig_ready, 1)
                if s.load_next:
                    x_upper(s.k + 1, 0)
                if s.c:
                    relus(s, 0)
                if s.c_next and s.b != 4:
                    upper(s)
                for c in {2: (0, 1), 3: (2, 3), 4: (4, 5)}.get(s.b, ()):
                    chunk_means(s, c)
                if s.a:
                    for o in range(CT):
                        act.wait_ge(f_psum, CT * s.k + o + 1)
                        nc.scalar.activation(fused[:, o, ring(s.k)], pf[o][:, 0:PX], ACT.Relu,
                                             bias=bias1[:, o:o + 1]).then_inc(f_ready, 1)
                if s.b == 4:
                    chunk_means(s, 6)
                    chunk_means(s, 7)
                if s.c:
                    relus(s, 1)
                if s.load_next:
                    x_upper(s.k + 1, 1)
                if s.b == 4:
                    act.wait_ge(hid_psum, s.nb + 1)
                    nc.scalar.activation(hid[:, :], pm[:, 0:2], ACT.Relu).then_inc(hid_ready, 1)
                    act.wait_ge(logit_ready, s.nb + 1)
                    nc.scalar.activation(ch[:, :], logit[:, :], ACT.Sigmoid).then_inc(ch_ready, 1)
                    act.wait_ge(ch_ready, s.nb + 1)
                    upper(s)

            slots(act, body)

        @block.vector
        def _(dve):
            steps = [0]

            def link(ins):
                steps[0] += 1
                ins.then_inc(dve_step, 1)
                dve.wait_ge(dve_step, steps[0])

            dve.wait_ge(v_landed, 160)
            nc.vector.tensor_scalar(t1[:, 0, 0:CT], v1[:, 4, :], EPS, None, ALU.add).then_inc(var_ready, 1)
            nc.vector.tensor_scalar(t1[:, 0, CT:], v2[:, 4, :], EPS, None, ALU.add).then_inc(var_ready, 1)
            dve.wait_ge(var_ready, 2)
            dve.wait_ge(root_ready, 1)
            link(nc.vector.reciprocal(t1[:, 2, :], t1[:, 1, :]))
            link(nc.vector.tensor_tensor(t1[:, 2, :], t1[:, 2, :], t1[:, 0, :], ALU.mult))
            link(nc.vector.scalar_tensor_tensor(t1[:, 1, :], t1[:, 1, :], 0.0, t1[:, 2, :], ALU.add, ALU.add))
            link(nc.vector.tensor_scalar(t1[:, 1, :], t1[:, 1, :], 0.5, None, ALU.mult))
            link(nc.vector.reciprocal(t1[:, 2, :], t1[:, 1, :]))
            for v, cols in ((v1, slice(0, CT)), (v2, slice(CT, CT + NB))):
                link(nc.vector.tensor_tensor(t1[:, 2, cols], t1[:, 2, cols], v[:, 1, :], ALU.mult))
                link(nc.vector.tensor_tensor(t1[:, 3, cols], v[:, 0, :], v[:, 3, :], ALU.subtract))
                link(nc.vector.tensor_tensor(t1[:, 3, cols], t1[:, 3, cols], t1[:, 2, cols], ALU.mult))
                link(nc.vector.tensor_tensor(t1[:, 3, cols], t1[:, 3, cols], v[:, 2, :], ALU.add))
            link(nc.vector.tensor_scalar(t1[:, 2, :], t1[:, 2, :], 0.5, None, ALU.mult))

            dve.wait_ge(w_landed, 16)
            for o in range(CT):
                w = tmp if o == 0 else tmp2
                link(nc.vector.tensor_scalar(w[:, :, :], fw[:, o, :, :], t1[:, 2, o:o + 1], None, ALU.mult))
                for j in range(2):
                    nc.vector.tensor_tensor(fw[:, o, 2 * j, :], w[:, 2 * j, :], w[:, 2 * j + 1, :], ALU.add)
                    ins = nc.vector.tensor_tensor(fw[:, o, 2 * j + 1, :], w[:, 2 * j, :], w[:, 2 * j + 1, :],
                                                  ALU.subtract)
                link(ins)
                for r in range(2):
                    nc.vector.tensor_tensor(fh[:, o, 2 * r, :], fw[:, o, r, :], fw[:, o, 2 + r, :], ALU.add
                                            ).then_inc(fh_ready, 1)
                    ins = nc.vector.tensor_tensor(fh[:, o, 2 * r + 1, :], fw[:, o, r, :], fw[:, o, 2 + r, :],
                                                  ALU.subtract)
                    ins.then_inc(fh_ready, 1)

            for q in range(4):
                dve.wait_ge(wfhi_ready, q + 1)
                nc.vector.tensor_tensor(wf_lo[:, :, q, :], pp[q][:, :].rearrange("p (i o) -> p i o", i=CT),
                                        wf_hi[:, :, q, :].bitcast(F32), ALU.subtract).then_inc(wflo_ready, 1)

            dve.wait_ge(w_landed, 32)
            for t in range(NB):
                ins = nc.vector.tensor_scalar(pw[:, t, :], pw[:, t, :], t1[:, 2, CT + t:CT + t + 1], None, ALU.mult)
            ins.then_inc(pw_ready, 1)
            link(nc.vector.tensor_scalar(bias2, bias2, 0.5, None, ALU.mult))
            nc.vector.tensor_scalar(nbias2[:, :], bias2, -1.0, None, ALU.mult).then_inc(bias_ready, 1)
            ll, hl = bias2[:, LL * CT:LL * CT + CT], bias2[:, HL * CT:HL * CT + CT]
            nc.vector.tensor_tensor(both[:, 0, :], ll, hl, ALU.add).then_inc(bias_ready, 1)
            nc.vector.tensor_tensor(both[:, 1, :], ll, hl, ALU.subtract).then_inc(bias_ready, 1)
            dve.wait_ge(bias_ready, 3)
            for q in range(4):
                dve.wait_ge(wphi_ready, q + 1)
                bank = pf[q][:, :] if q < 2 else pm[:, (q - 2) * 512:(q - 1) * 512]
                cols = slice((q % 2) * 512, (q % 2 + 1) * 512)
                nc.vector.tensor_tensor(wp_lo[:, q // 2, cols], bank, wp_hi[:, q // 2, cols].bitcast(F32),
                                        ALU.subtract).then_inc(wplo_ready, 1)

            for i in range(CT):
                x_lower(dve, nc.vector, 0, i)

            def bands(dx):
                for j in range(NK):
                    tap = taps[:, bass.ds(j * KS + dx, 1)]
                    eye = eye_pad[:, bass.ds(dx, W2)]
                    if isinstance(dx, int):
                        ins = nc.vector.tensor_scalar(band[:, j, :], eye, tap, None, ALU.mult)
                    else:
                        if j == 0:
                            dve.wait_ge(band_pass, NK * dx)
                        ins = nc.vector.scalar_tensor_tensor(band[:, j, :], eye, tap, band[:, j, :],
                                                             ALU.mult, ALU.add)
                    ins.then_inc(band_pass, 1)

            def butterflies(s, i):
                g = 2 * s.kc + i
                for n, j in enumerate((LL, HL)):
                    dve.wait_ge(p_psum, 4 * g + 2 + 2 * n)
                    dve.wait_ge(r_ready, 2 * g + 1 + n)
                    rows = sd[:, n, :].rearrange("p (y r w) -> p y r w", r=2, w=W2)
                    p = pp[j][:, 0:PX].rearrange("p (y w) -> p y w", w=W2)
                    q = relu[:, n, :].rearrange("p (y w) -> p y w", w=W2)
                    need(dve, cell_ready, 2 * g)
                    low = nbias2[:, j * CT + i:j * CT + i + 1]
                    nc.vector.scalar_tensor_tensor(rows[:, :, 0, :], p, low, q, ALU.max, ALU.add
                                                   ).then_inc(sd_ready, 1)
                    nc.vector.scalar_tensor_tensor(rows[:, :, 1, :], p, low, q, ALU.max, ALU.subtract
                                                   ).then_inc(sd_ready, 1)

            def cells(s, i):
                g = 2 * s.kc + i
                dve.wait_ge(sd_ready, 4 * (g + 1))
                need(dve, add_done, g - 1 if s.pool_adds_prev or s.pool_adds and i else g)
                px = cells_of(s.pool_adds, i).rearrange("p (y w c) -> p y w c", w=W2, c=2)
                s0 = sd[:, 0, :].rearrange("p (y w) -> p y w", w=W2)
                s1 = sd[:, 1, :].rearrange("p (y w) -> p y w", w=W2)
                for c, op in enumerate((ALU.add, ALU.subtract)):
                    nc.vector.scalar_tensor_tensor(px[:, :, :, c], s0, both[:, c, i:i + 1], s1, ALU.add, op
                                                   ).then_inc(cell_ready, 1)

            def chunk_max(s, c):
                dve.wait_ge(mult_done, CT * (NCH * s.nb + c + 1))
                nc.vector.tensor_reduce(part[:, 1, :, c], fused[:, :, ring(TILES * s.nb + CHUNK * c, CHUNK)],
                                        AX.X, ALU.max).then_inc(cmax_done, 1)

            def lower(s):
                dve.wait_ge(hi_ready, CT * (s.kn + 1))
                for i in range(CT):
                    nc.vector.scalar_tensor_tensor(y_lo[:, s.pn, i, :], fused[:, i, ring(s.kn + RING)],
                                                   ch[:, i:i + 1], y_hi[:, s.pn, i, :].bitcast(F32),
                                                   ALU.mult, ALU.subtract).then_inc(lo_ready, 1)

            def body(s):
                if s.load_next:
                    x_lower(dve, nc.vector, s.k + 1, 0)
                if s.c:
                    butterflies(s, 0)
                    if not s.c_is_first and not s.pool_adds_prev:
                        residual(dve, nc.vector, s.mc_prev, s.pn, 1, 2 * s.kc - 1, cells_of(False, 1))
                    cells(s, 0)
                if s.a:
                    dve.wait_ge(f_ready, CT * (s.k + 1))
                    need(dve, t_psum, s.k - 1)
                    nc.vector.tensor_tensor(mx[:, s.u, :], fused[:, 0, ring(s.k)], fused[:, 1, ring(s.k)],
                                            ALU.max).then_inc(mx_ready, 1)
                if s.turn:
                    dve.wait_ge(t_psum, s.k)
                    _, t = s.tile(1)
                    nc.vector.tensor_reduce(maps[:, 1, bass.ds(t * ROWS + PAD, ROWS)],
                                            pm[0:W2, 0:ROWS * P].rearrange("p (r c) -> p r c", r=ROWS),
                                            AX.X, ALU.max).then_inc(map_ready, 1)
                    nc.vector.tensor_scalar(maps[:, 0, bass.ds(t * ROWS + PAD, ROWS)],
                                            pm[0:W2, MEANS:MEANS + ROWS], 1.0 / C, None, ALU.mult
                                            ).then_inc(map_ready, 1)
                if s.c_next and s.b != 4:
                    lower(s)
                if s.c:
                    butterflies(s, 1)
                if s.b == 4:
                    chunk_max(s, 6)
                    chunk_max(s, 7)
                    dve.wait_ge(csum_done, CT * NCH * (s.nb + 1))
                    dve.wait_ge(cmax_done, NCH * (s.nb + 1))
                    nc.vector.tensor_reduce(pool[:, :, 0], part[:, 0, :, :], AX.X, ALU.add).then_inc(pool_ready, 1)
                    nc.vector.tensor_reduce(pool[:, :, 1], part[:, 1, :, :], AX.X, ALU.max).then_inc(pool_ready, 1)
                if s.c:
                    if not s.pool_adds:
                        residual(dve, nc.vector, s.mc, s.pc, 0, 2 * s.kc, cells_of(False, 0))
                    cells(s, 1)
                if s.load_next and not s.c:
                    x_lower(dve, nc.vector, s.k + 1, 1)
                if s.band_dx is not None:
                    bands(s.band_dx)
                for c in {1: (0, 1), 2: (2, 3), 3: (4, 5)}.get(s.b, ()):
                    chunk_max(s, c)
                if s.b == 4:
                    dve.wait_ge(logit_psum, s.nb + 1)
                    nc.vector.tensor_reduce(logit[:, :], pm[:, 512:516].rearrange("p (i v) -> p i v", i=CT),
                                            AX.X, ALU.add).then_inc(logit_ready, 1)
                    lower(s)

            dve.wait_ge(taps_landed, 16)
            dve.wait_ge(ident_ready, 2)
            slots(dve, body)


_INS = ["x"] + ["L0_conv_" + n for n in (
    "fusion_w", "fusion_b", "bn1_g", "bn1_b", "bn1_m", "bn1_v", "sa_w", "ca_w1", "ca_w2",
    "proj_w", "proj_b", "bn2_g", "bn2_b", "bn2_m", "bn2_v")]


def kernel(**inputs):
    import numpy as _np
    import concourse.bacc as _bacc
    from concourse import mybir as _mybir
    from concourse.bass_utils import run_bass_kernel_spmd as _run

    nc = _bacc.Bacc("TRN2", target_bir_lowering=False, num_devices=1, dynamic_dma_scratch_size=1024)
    arrays, args = {}, []
    for name in _INS:
        a = _np.ascontiguousarray(inputs[name])
        arrays[f"in_{name}_dram"] = a
        args.append(nc.dram_tensor(f"in_{name}_dram", a.shape, _mybir.dt.from_np(a.dtype), kind="ExternalInput").ap())
    shape = inputs["x"].shape
    args.append(nc.dram_tensor("out_0_dram", shape, _mybir.dt.float32, kind="ExternalOutput").ap())
    haar_block(nc, *args)
    r = _run(nc, [arrays], core_ids=[0])
    return r.results[0]["out_0_dram"]
```
